# Optimizing a Trainium2 kernel written in Bass

```python
import numpy as np
import jax
import jax.numpy as jnp

def _softmax(x, axis=-1):
    return jax.nn.softmax(x, axis=axis)

def _gelu(x):
    return jax.nn.gelu(x, approximate=True)

def _silu(x):
    return jax.nn.silu(x)

def _sigmoid(x):
    return jax.nn.sigmoid(x)

def _layernorm(x, axis=-1, eps=1e-05):
    m = jnp.mean(x, axis=axis, keepdims=True)
    v = jnp.var(x, axis=axis, keepdims=True)
    return (x - m) / jnp.sqrt(v + eps)

def _scatter_add(tgt, idx, src, axis=0):
    return tgt.at[idx].add(src)

def _segment_sum(src, seg, n):
    return jax.ops.segment_sum(src, seg, n)
kernel_name = 'mk_adaln_ffn_d2_seqx_r4_67f55d'

def setup_inputs(seed: int=0):
    np.random.seed(seed)
    _w = jnp.asarray

    def _rec_inputs():
        import jax
        import jax.numpy as jnp
        _rk = jax.random.key(seed)
        x = -0.000125 + 0.9999 * jax.random.normal(jax.random.fold_in(_rk, 1), (64, 64, 1024), jnp.float32)
        _lenS = 64 - jax.random.randint(jax.random.fold_in(_rk, 7), (64,), 0, max(1, 64 // 4) + 1, jnp.int32)
        _lenS2 = 64 - jax.random.randint(jax.random.fold_in(_rk, 8), (64,), 0, max(1, 64 // 4) + 1, jnp.int32)
        condB_codebook = -0.0625 + 0.715345 * jax.random.normal(jax.random.fold_in(_rk, 11), (64,), jnp.float32)
        itok_B_1_7 = jax.random.randint(jax.random.fold_in(_rk, 12), (64,), 1, 8, jnp.int32)
        return (x, condB_codebook, itok_B_1_7)
    x, condB_codebook, itok_B_1_7 = _rec_inputs()

    def _L0_cond_setup():
        import jax, jax.numpy as jnp
        import numpy as np
        GROUP = 128
        LORA_ALPHA = 32.0
        LORA_RANK = 64
        key = jax.random.key(seed)
        k1, k2, k3, k4 = jax.random.split(key, 4)
        O, I = (1024, 1024)
        x = jax.random.normal(k1, (4, 512, I), dtype=jnp.float32)
        weight = jax.random.normal(k2, (O, I), dtype=jnp.float32) * 0.02
        wg = weight.reshape(O, I // GROUP, GROUP)
        scale_log = jnp.log(jnp.clip(jnp.max(jnp.abs(wg), axis=2, keepdims=True), 1e-05))
        codebook = jnp.array([-1.0, -0.25, 0.0, 1.0], dtype=jnp.float32)
        lora_A = jax.random.normal(k3, (LORA_RANK, I), dtype=jnp.float32) * 0.02
        lora_B = jax.random.normal(k4, (O, LORA_RANK), dtype=jnp.float32) * 0.02
        return {'x': x, 'weight': weight, 'scale_log': scale_log, 'codebook': codebook, 'lora_A': lora_A, 'lora_B': lora_B}
    _L0_cond_all = _L0_cond_setup()
    _L0_cond_in = {k: v for k, v in _L0_cond_all.items() if k in ('weight', 'scale_log', 'lora_A', 'lora_B')}
    del _L0_cond_all

    def _L0_ffn_setup():
        import jax, jax.numpy as jnp
        import numpy as np
        NUM_EXPERTS = 8
        TOP_K = 2
        RANK = 16
        LORA_ALPHA = 32
        SCALING = LORA_ALPHA / RANK
        key = jax.random.key(seed)
        ks = jax.random.split(key, 6)
        B, S, D_IN, D_OUT = (4, 512, 1024, 1024)
        x = jax.random.normal(ks[0], (B, S, D_IN), dtype=jnp.float32)
        W_base = jax.random.normal(ks[1], (D_OUT, D_IN), dtype=jnp.float32) * 0.02
        b_base = jax.random.normal(ks[2], (D_OUT,), dtype=jnp.float32) * 0.02
        W_router = jax.random.normal(ks[3], (NUM_EXPERTS, D_IN), dtype=jnp.float32) * 0.02
        A = jax.random.normal(ks[4], (NUM_EXPERTS, RANK, D_IN), dtype=jnp.float32) * 0.02
        Bm = jax.random.normal(ks[5], (D_OUT, RANK), dtype=jnp.float32) * 0.02
        Bm = jnp.broadcast_to(Bm, (NUM_EXPERTS, D_OUT, RANK)) * jnp.arange(1, NUM_EXPERTS + 1, dtype=jnp.float32)[:, None, None] * 0.2
        return {'x': x, 'W_base': W_base, 'b_base': b_base, 'W_router': W_router, 'A': A, 'B': Bm}
    _L0_ffn_all = _L0_ffn_setup()
    _L0_ffn_in = {k: v for k, v in _L0_ffn_all.items() if k in ('W_base', 'b_base', 'W_router', 'A', 'B')}
    del _L0_ffn_all

    def _L1_cond_setup():
        import jax, jax.numpy as jnp
        import numpy as np
        B, S, D_IN, D_OUT = (4, 512, 1024, 1024)
        N_ADAPTERS, MAX_RANK = (8, 16)
        key = jax.random.key(seed)
        ks = jax.random.split(key, 7)
        x = jax.random.normal(ks[0], (B, S, D_IN), dtype=jnp.float32)
        weight = jax.random.normal(ks[1], (D_OUT, D_IN), dtype=jnp.float32) * (1.0 / np.sqrt(D_IN))
        bias = jax.random.normal(ks[2], (D_OUT,), dtype=jnp.float32) * 0.01
        lora_a_weights = jax.random.normal(ks[3], (N_ADAPTERS, MAX_RANK, D_IN), dtype=jnp.float32) * (1.0 / np.sqrt(D_IN))
        lora_b_weights = jax.random.normal(ks[4], (N_ADAPTERS, D_OUT, MAX_RANK), dtype=jnp.float32) * 0.02
        scaling_factors = jax.random.uniform(ks[5], (N_ADAPTERS,), dtype=jnp.float32, minval=0.5, maxval=2.0)
        adapter_id = jax.random.randint(ks[6], (B,), 0, N_ADAPTERS, dtype=jnp.int64)
        return {'x': x, 'weight': weight, 'bias': bias, 'lora_a_weights': lora_a_weights, 'lora_b_weights': lora_b_weights, 'scaling_factors': scaling_factors, 'adapter_id': adapter_id}
    _L1_cond_all = _L1_cond_setup()
    _L1_cond_in = {k: v for k, v in _L1_cond_all.items() if k in ('weight', 'bias', 'lora_a_weights', 'lora_b_weights', 'scaling_factors')}
    del _L1_cond_all

    def _L1_ffn_setup():
        import jax, jax.numpy as jnp
        import numpy as np
        R = 16
        ALPHA = 32
        SCALING = ALPHA / R
        E = 8
        TOP_K = 2
        key = jax.random.key(seed)
        ks = jax.random.split(key, 5)
        B, S, D = (4, 512, 1024)
        x = jax.random.normal(ks[0], (B, S, D), dtype=jnp.float32)
        base_W = jax.random.normal(ks[1], (D, D), dtype=jnp.float32) * 0.02
        router_W = jax.random.normal(ks[2], (E, D), dtype=jnp.float32) * 0.02
        lora_A = jax.random.normal(ks[3], (E, D, R), dtype=jnp.float32) * 0.02
        lora_B = jax.random.normal(ks[4], (E, R, D), dtype=jnp.float32) * 0.02
        return {'x': x, 'base_W': base_W, 'router_W': router_W, 'lora_A': lora_A, 'lora_B': lora_B}
    _L1_ffn_all = _L1_ffn_setup()
    _L1_ffn_in = {k: v for k, v in _L1_ffn_all.items() if k in ('base_W', 'router_W', 'lora_A', 'lora_B')}
    del _L1_ffn_all
    return {'x': x, 'condB_codebook': condB_codebook, 'itok_B_1_7': itok_B_1_7, 'L0_cond_weight': _L0_cond_in['weight'], 'L0_cond_scale_log': _L0_cond_in['scale_log'], 'L0_cond_lora_A': _L0_cond_in['lora_A'], 'L0_cond_lora_B': _L0_cond_in['lora_B'], 'L0_ffn_W_base': _L0_ffn_in['W_base'], 'L0_ffn_b_base': _L0_ffn_in['b_base'], 'L0_ffn_W_router': _L0_ffn_in['W_router'], 'L0_ffn_A': _L0_ffn_in['A'], 'L0_ffn_B': _L0_ffn_in['B'], 'L1_cond_weight': _L1_cond_in['weight'], 'L1_cond_bias': _L1_cond_in['bias'], 'L1_cond_lora_a_weights': _L1_cond_in['lora_a_weights'], 'L1_cond_lora_b_weights': _L1_cond_in['lora_b_weights'], 'L1_cond_scaling_factors': _L1_cond_in['scaling_factors'], 'L1_ffn_base_W': _L1_ffn_in['base_W'], 'L1_ffn_router_W': _L1_ffn_in['router_W'], 'L1_ffn_lora_A': _L1_ffn_in['lora_A'], 'L1_ffn_lora_B': _L1_ffn_in['lora_B']}

def reference(x, condB_codebook, itok_B_1_7, L0_cond_weight, L0_cond_scale_log, L0_cond_lora_A, L0_cond_lora_B, L0_ffn_W_base, L0_ffn_b_base, L0_ffn_W_router, L0_ffn_A, L0_ffn_B, L1_cond_weight, L1_cond_bias, L1_cond_lora_a_weights, L1_cond_lora_b_weights, L1_cond_scaling_factors, L1_ffn_base_W, L1_ffn_router_W, L1_ffn_lora_A, L1_ffn_lora_B):
    import jax
    import jax.numpy as jnp

    def _L0_cond_ref(x, weight, scale_log, codebook, lora_A, lora_B):
        import jax, jax.numpy as jnp
        import numpy as np
        GROUP = 128
        LORA_ALPHA = 32.0
        LORA_RANK = 64
        O, I = weight.shape
        lora_delta = lora_B @ lora_A * (LORA_ALPHA / LORA_RANK)
        cb = codebook / jnp.clip(jnp.max(jnp.abs(codebook)), 1e-08)
        scale = jnp.exp(scale_log)
        wg = (weight + lora_delta).reshape(O, I // GROUP, GROUP)
        normalized = wg / scale
        thresholds = (cb[:-1] + cb[1:]) * 0.5
        idx = jnp.searchsorted(thresholds, normalized, side='left')
        quantized = cb[idx]
        w = jax.lax.stop_gradient(quantized - normalized) + normalized
        w_q = (w * scale).reshape(O, I)
        w_eff = w_q + lora_delta
        return x @ w_eff.T

    def _L0_ffn_ref(x, W_base, b_base, W_router, A, B):
        import jax, jax.numpy as jnp
        import numpy as np
        NUM_EXPERTS = 8
        TOP_K = 2
        RANK = 16
        LORA_ALPHA = 32
        SCALING = LORA_ALPHA / RANK
        bs, seq, d_in = x.shape
        T = bs * seq
        xf = x.reshape(T, d_in)
        base = xf @ W_base.T + b_base
        logits = xf @ W_router.T
        rw, sel = jax.lax.top_k(logits, TOP_K)
        rw = jax.nn.softmax(rw, axis=-1)
        onehot = jax.nn.one_hot(sel, NUM_EXPERTS, dtype=rw.dtype)
        w = jnp.einsum('tk,tke->te', rw, onehot)
        h = jnp.einsum('td,erd->ter', xf, A)
        lora = jnp.einsum('ter,te,eor->to', h, w, B) * SCALING
        return (base + lora).reshape(bs, seq, -1)

    def _L1_cond_ref(x, weight, bias, lora_a_weights, lora_b_weights, scaling_factors, adapter_id):
        import jax, jax.numpy as jnp
        import numpy as np
        B, S, D_IN, D_OUT = (4, 512, 1024, 1024)
        N_ADAPTERS, MAX_RANK = (8, 16)
        base = jnp.einsum('bsi,oi->bso', x, weight) + bias
        a_sel = lora_a_weights[adapter_id]
        b_sel = lora_b_weights[adapter_id]
        scale = scaling_factors[adapter_id]
        low = jnp.einsum('bsi,bri->bsr', x, a_sel)
        delta = jnp.einsum('bsr,bor->bso', low, b_sel)
        return base + scale[:, None, None] * delta

    def _L1_ffn_ref(x, base_W, router_W, lora_A, lora_B):
        import jax, jax.numpy as jnp
        import numpy as np
        R = 16
        ALPHA = 32
        SCALING = ALPHA / R
        E = 8
        TOP_K = 2
        base = jnp.einsum('bsd,od->bso', x, base_W)
        logits = jnp.einsum('bsd,ed->bse', x, router_W)
        probs = jax.nn.softmax(logits.astype(jnp.float32), axis=-1)
        top_vals, top_idx = jax.lax.top_k(probs, TOP_K)
        rw = top_vals / jnp.sum(top_vals, axis=-1, keepdims=True)
        w_dense = jnp.sum(jax.nn.one_hot(top_idx, E, dtype=rw.dtype) * rw[..., None], axis=-2).astype(x.dtype)
        mid = jnp.einsum('bsd,edr->bser', x, lora_A)
        mid = mid * w_dense[..., None]
        inc = jnp.einsum('bser,erd->bsd', mid, lora_B)
        return base + inc * SCALING
    x = x + _L0_ffn_ref(_L0_cond_ref(x, L0_cond_weight, L0_cond_scale_log, condB_codebook, L0_cond_lora_A, L0_cond_lora_B), L0_ffn_W_base, L0_ffn_b_base, L0_ffn_W_router, L0_ffn_A, L0_ffn_B)
    x = x + _L1_ffn_ref(_L1_cond_ref(x, L1_cond_weight, L1_cond_bias, L1_cond_lora_a_weights, L1_cond_lora_b_weights, L1_cond_scaling_factors, itok_B_1_7), L1_ffn_base_W, L1_ffn_router_W, L1_ffn_lora_A, L1_ffn_lora_B)
    return x

_drawn_inputs = setup_inputs


def setup_inputs(seed=0):
    import zlib

    import numpy as np

    out = dict(_drawn_inputs(seed))
    spreads = {}
    factors = {'L0_ffn_b_base': 3.32, 'L1_cond_bias': 4.843, 'L1_cond_scaling_factors': 2.675}
    for name, (base, spread) in spreads.items():
        noise = np.random.default_rng([zlib.crc32(name.encode()), seed]).standard_normal(out[name].shape)
        drawn = base * np.exp(spread * noise) if base else spread * noise
        out[name] = jnp.asarray(drawn.astype(out[name].dtype))
    for name, factor in factors.items():
        out[name] = (out[name] * factor).astype(out[name].dtype)
    return out
```

```python
from contextlib import ExitStack

import numpy as np
import concourse.bass as bass
from concourse import mybir

F32 = mybir.dt.float32
F32R = mybir.dt.float32r
I32 = mybir.dt.int32
ALU = mybir.AluOpType
ACT = mybir.ActivationFunctionType
AX_X = mybir.AxisListType.X

P = 128
D = 1024
KC = D // P
T = 4096
TT = 512
NT = T // TT
SEQ = 64
E = 8
ER = P
GRP = 128
LV = 64
NF = 7
NM1 = D + ER + E
NE = D + 2 * ER + E
LOW0, MID0, LG0 = D, D + ER, D + 2 * ER
GM = D + 2 * ER
NX0 = E + ER
NGX = 2 * E + ER
NGL = 4 * E
NB, BW = 4, NE // 4
NR = 6
E_OUT_AT = {True: {NF - 2: 0, NF - 3: 1, NF - 4: 2}, False: {NF - 2: 0, NF - 4: 1, NF - 5: 2}}
VS_ACT = 6
B0_BANKS = [3, 0, 1, 2]
A_COLS = [(0, 388), (388, 388), (776, 384)]
C_ID, C_REV, C_NIDX, C_TRI, C_IOTA, C_SEL, C_SLOG, C_B0, C_B1, C_SF, C_END = \
    0, 128, 160, 162, 226, 290, 306, 370, 378, 386, 387
BIG = 3.0e38


def build(nc, xT, w1, m1t, aallt, bl1, wbt, x0t, b0t, lb1, lorabt, loraa, wq, cbook, ids, packed, out,
          e_dram, p1_dram):
    with ExitStack() as ctx:
        base = (nc.sbuf_base + 31) // 32 * 32
        r1 = base
        r2 = r1 + KC * (GM + NGX) * 8
        r4 = r2 + KC * D * 8

        def at(name, shape, dt, offset):
            return nc.alloc_sbuf_tensor_at(name, shape, dt, offset=offset)

        def bank(name):
            return ctx.enter_context(nc.psum_tensor(name, [P, 512], F32))

        def sem(name):
            return ctx.enter_context(nc.semaphore(name))

        weff_hi = at("weff_hi", [P, KC, D], F32R, r1)
        weff_lo = at("weff_lo", [P, KC, D], F32R, r1 + 32768)
        qbuf = [at(f"qbuf{u}", [P, D], F32, r1 + 65536 + 4096 * u) for u in range(2)]
        rbuf = [at(f"rbuf{u}", [P, D], F32, r1 + 73728 + 4096 * u) for u in range(2)]
        m1_raw = [at(f"m1_raw{c}", [P, NM1], F32, r1 + (4640 * c if c < 7 else 32768)) for c in range(KC)]
        wq_sb = [at("wq_sb0", [P, D], F32, r1 + 86560), at("wq_sb1", [P, D], F32, r2 + KC * D * 8 + 41728)]
        bl1_raw = at("bl1_raw", [P, KC, ER], F32, r1 + 81920)
        bl1_hi = at("bl1_hi", [P, KC, ER], F32R, r2 + KC * D * 8 + 41728)
        bl1_lo = at("bl1_lo", [P, KC, ER], F32R, r1 + 86560)
        x0_hl = at("x0_hl", [P, KC, 2 * NX0], F32R, r1 + 65536)
        x0_raw = at("x0_raw", [P, KC, NX0], F32, r1 + 74240)
        g_hi = at("g_hi", [P, KC, GM], F32R, r1)
        g_lo = at("g_lo", [P, KC, GM], F32R, r1 + 40960)
        gx = at("gx", [P, KC, NGL + ER], F32R, r1 + 81920)
        h0_lo = at("h0_lo", [P, KC, ER], F32R, r1 + 87040)
        tr = r1 + 61440
        m1_hi = at("m1_hi", [P, KC, NM1], F32R, r2)
        m1_lo = at("m1_lo", [P, KC, NM1], F32R, r2 + 37120)
        c0_hi = at("c0_hi", [P, KC, D], F32R, r2)
        c0_lo = at("c0_lo", [P, KC, D], F32R, r2 + 32768)
        x_hi = [at(f"x_hi{u}", [P, KC, TT], F32R, r2 + 32768 * u) for u in range(2)]
        x_lo = [at(f"x_lo{u}", [P, KC, TT], F32R, r2 + 32768 * u + 16384) for u in range(2)]
        w_raw = [at(f"w_raw{u}", [P, KC, P], F32, r4 + 8704 + 4096 * u) for u in range(2)]
        w_hi = [at(f"w_hi{u}", [P, KC, P], F32R, r4 + 16896 + 4096 * u) for u in range(2)]
        w_lo = [at(f"w_lo{u}", [P, KC, P], F32R, r4 + 25088 + 4096 * u) for u in range(2)]
        est = at("est", [P, NM1], F32, r4 + 33280)
        bacc = at("bacc", [P, NE], F32, r4 + 41728)
        loraa_sb = at("loraa_sb", [64, D], F32, r4 + 46880)
        lorab_sb = [at(f"lorab_sb{u}", [64, P], F32, r4 + 50976 + 512 * u) for u in range(2)]
        tmp = [at(f"tmp{u}", [P, D], F32, r4 + 4096 * u) for u in range(2)]
        p0 = at("p0", [P, 2 * NE], F32R, r4)
        p0_hi, p0_lg, p0_lo = p0[:, 0:NE], p0[:, LG0:NE + E], p0[:, NE + E:2 * NE]
        hx = [at(f"hx{b}", [P, NX0], F32, r4 + 8192 + 544 * b) for b in range(2)]
        eb_hi = at("eb_hi", [P, KC, BW], F32R, r4 + 10304)
        eb_lo = at("eb_lo", [P, KC, BW], F32R, r4 + 20608)
        e_raw = [at(f"e_raw{b}", [P, BW], F32, r4 + (30912 + 1312 * b if b < 2 else 46880 + 1312 * (b - 2)))
                 for b in range(NR)]
        b0t_hi = at("b0t_hi", [P, KC, ER], F32R, r4 + 33536)
        b0t_lo = at("b0t_lo", [P, KC, ER], F32R, r4 + 37632)
        b0t_raw = at("b0t_raw", [P, KC, ER], F32, r1 + 74240)
        m1_again = [est, at("m1_again", [P, NM1], F32, r4 + 46880)]
        p1 = at("p1", [P, 2 * NM1], F32R, r4 + 10304)
        p1_hi, p1_lg, p1_lo = p1[:, 0:NM1], p1[:, NM1 - E:NM1 + E], p1[:, NM1 + E:2 * NM1]
        lb1_hi = at("lb1_hi", [P, D], F32R, r4 + 19584)
        lb1_lo = at("lb1_lo", [P, D], F32R, r4 + 23680)
        x_raw = [at(f"x_raw{b}", [P, TT], F32, r4 + 48256 + 2048 * b) for b in range(2)]
        x_first = [at(f"x_first{c}", [P, TT], F32, r4 + (30912 if c == 2 else 33536 + 2048 * (c - 3)))
                   for c in range(2, KC - 1)]
        x_first = [*x_raw, *x_first, x_raw[1]]
        names = ("m0", "low", "mid")
        mv_hi = {n: at(f"{n}_hi", [P, TT], F32R, r4 + 27776 + 4096 * i) for i, n in enumerate(names)}
        mv_lo = {n: at(f"{n}_lo", [P, TT], F32R, r4 + 29824 + 4096 * i) for i, n in enumerate(names)}
        lb1_raw = at("lb1_raw", [P, D], F32, r4 + 27776)
        p1_raw = at("p1_raw", [P, NM1], F32, r4 + 40064)
        lg_sb = at("lg_sb", [NGL, TT], F32, r4 + 40064)
        wx_sb = at("wx_sb", [P, TT], F32, r4 + 40064)
        mraw = at("mraw", [P, TT], F32, r4 + 42112)
        wrep = at("wrep", [P, TT], F32, r4 + 42112)
        ost = [at(f"ost{b}", [P, TT], F32, r4 + 44160 + 2048 * b) for b in range(2)]

        small_at = [r4 + 52352]

        def small(name, shape, dt=F32):
            n = 4 * int(np.prod(shape[1:]))
            h = at(name, shape, dt, small_at[0])
            small_at[0] += (n + 31) // 32 * 32
            assert small_at[0] <= nc.sbuf_usable_end
            return h

        pk = small("pk", [P, C_END])
        ident = pk[:, C_ID:C_ID + P]
        rev = pk[:, C_REV:C_REV + 32].rearrange("p (s e) -> p s e", e=E)
        nidx, sfc = pk[:, C_NIDX:C_NIDX + 1], pk[:, C_SF:C_SF + 1]
        tri, iota = pk[0:LV, C_TRI:C_TRI + LV], pk[0:LV, C_IOTA:C_IOTA + LV]
        sel = [pk[0:NGL, C_SEL:C_SEL + E], pk[0:2 * E, C_SEL + E:C_SEL + 2 * E]]
        slog = pk[:, C_SLOG:C_SLOG + 64]
        b0c, b1c = pk[:, C_B0:C_B0 + KC], pk[:, C_B1:C_B1 + KC]
        scale = small("scale", [P, KC * KC])
        rscale = small("rscale", [P, KC * KC])
        vscale = at("vscale", [P, KC * KC], F32, r4 + 37920)
        mask_s = small("mask_s", [P, T // SEQ])
        thr = small("thr", [P, LV])
        step = small("step", [P, LV])
        biasv = small("biasv", [P, 16])
        cnt = small("cnt", [P, 2], I32)
        val0 = small("val0", [P, 1])
        rt = [small(f"rt{i}", [P, 4, E]) for i in range(4)]
        rs4 = [small(f"rs4_{i}", [P, 4]) for i in range(6)]
        ones = small("ones", [P, 2])

        def row(name, shape, dt=F32):
            h = at(name, shape, dt, tr_at[0])
            tr_at[0] += (4 * int(np.prod(shape[1:])) + 31) // 32 * 32
            assert tr_at[0] <= r1 + 65536
            return h

        tr_at = [tr]
        cb = row("cb", [P, LV])
        tt_ = row("tt_", [P, LV + 1])
        reach = row("reach", [P, LV])
        cols = row("cols", [LV, 4])
        selm = row("selm", [LV, LV])
        vcomp = row("vcomp", [P, LV])
        valid = row("valid", [P, LV])
        idraw = row("idraw", [P, T // SEQ], I32)
        idf = row("idf", [P, T // SEQ])
        one1 = row("one1", [P, 1])
        ex_n, ex_r, ex_p = row("ex_n", [P, 64]), row("ex_r", [P, 64]), row("ex_p", [P, 64])
        ex_i = row("ex_i", [P, 64], I32)

        bk = [bank(f"bank{i}") for i in range(8)]

        ld_cb, ld_const = sem("ld_cb"), sem("ld_const")
        ld_m1 = [sem(f"ld_m1_{c}") for c in range(KC)]
        wd_ok = [sem(f"wd_ok{u}") for u in range(2)]
        ld_mb, mb_ok, bacc0 = [sem(f"ld_mb{u}") for u in range(2)], sem("mb_ok"), sem("bacc0")
        m1_hi_s, m1_lo_s = sem("m1_hi_s"), sem("m1_lo_s")
        ld_w = [sem(f"ld_w{u}") for u in range(2)]
        ld_q = [sem(f"ld_q{u}") for u in range(2)]
        ld_lorab = [sem(f"ld_lorab{u}") for u in range(2)]
        ld_bl = sem("ld_bl")
        bl_hi, bl_lo = sem("bl_hi"), sem("bl_lo")
        ws_hi = [sem(f"ws_hi{u}") for u in range(2)]
        ws_lo = [sem(f"ws_lo{u}") for u in range(2)]
        q_ok = [sem(f"q_ok{u}") for u in range(2)]
        d_mm = [sem(f"d_mm{u}") for u in range(2)]
        r_ready = [sem(f"r_ready{u}") for u in range(2)]
        a_ready = [sem(f"a_ready{u}") for u in range(2)]
        q_tail = sem("q_tail")
        rs_ok, vs_ok = sem("rs_ok"), sem("vs_ok")
        weff_raw = [sem(f"weff_raw{u}") for u in range(2)]
        we_hi = [sem(f"we_hi{u}") for u in range(2)]
        we_lo = [sem(f"we_lo{u}") for u in range(2)]
        e_mm = [sem(f"e_mm{u}") for u in range(2)]
        e_ev = [sem(f"e_ev{g}") for g in range(3)]
        e_diag = sem("e_diag")
        st_e = sem("st_e")
        st_low = sem("st_low")
        p1_mm, p1_ev, st_p1 = sem("p1_mm"), sem("p1_ev"), sem("st_p1")
        b_mm = [sem(f"b_mm{u}") for u in range(2)]
        b_ev = [sem(f"b_ev{u}") for u in range(2)]
        b_diag = [sem(f"b_diag{u}") for u in range(2)]
        c_hi = [sem(f"c_hi{u}") for u in range(2)]
        c_lo = [sem(f"c_lo{u}") for u in range(2)]
        ld_rw0, x0_hi_s, x0_lo_s = sem("ld_rw0"), sem("x0_hi_s"), sem("x0_lo_s")
        h_mm, h_cp, h_sum, h_hi, h_lo = sem("h_mm"), sem("h_cp"), sem("h_sum"), sem("h_hi"), sem("h_lo")
        ld_b0t, b0t_hi_s, b0t_lo_s = sem("ld_b0t"), sem("b0t_hi_s"), sem("b0t_lo_s")
        ld_e = [sem(f"ld_e{b}") for b in range(NR)]
        eb_hi_s, eb_lo_s = sem("eb_hi_s"), sem("eb_lo_s")
        e_used = [sem(f"e_used{b}") for b in range(NR)]
        g_mm, eb_free = sem("g_mm"), sem("eb_free")
        g_hi_s = sem("g_hi_s")
        g_lo_s = [sem(f"g_lo_s{b}") for b in range(3)]
        bias_mm, bias_ok = sem("bias_mm"), sem("bias_ok")
        ld_p1, ld_lb1 = sem("ld_p1"), sem("ld_lb1")
        f_hi, f_lo = sem("f_hi"), sem("f_lo")
        dve = sem("dve_step")
        cols_mm, cols_ok, sel_ok, comp_mm = sem("cols_mm"), sem("cols_ok"), sem("sel_ok"), sem("comp_mm")
        rank_mm = sem("rank_mm")
        ld_x = [sem(f"ld_x{b}") for b in range(2)]
        ld_xf = [sem(f"ld_xf{c}") for c in range(2, KC - 1)]
        xs_hi, xs_lo = sem("xs_hi"), sem("xs_lo")
        lx_mm, h0_mm, lgt_mm, wx_mm = sem("lx_mm"), sem("h0_mm"), sem("lgt_mm"), sem("wx_mm")
        low_mm, mid_mm, out_mm = sem("low_mm"), sem("mid_mm"), sem("out_mm")
        lg_ok, wx_ok = sem("lg_ok"), sem("wx_ok")
        dif_ok, rex_ok, w_ok = sem("dif_ok"), sem("rex_ok"), sem("w_ok")
        raw_ok = sem("raw_ok")
        v_hi, v_lo = sem("v_hi"), sem("v_lo")
        lg1_mm = sem("lg1_mm")
        ev = [sem(f"ev{b}") for b in range(2)]
        st_o = [sem(f"st_o{b}") for b in range(2)]

        cbook_b = cbook.rearrange("(a n) -> a n", a=1).to_broadcast([P, LV])
        ids_b = ids.rearrange("(a n) -> a n", a=1).to_broadcast([P, T // SEQ])
        chunked = lambda ap: ap.rearrange("(c p) n -> p c n", p=P)
        N_CONST = 3

        def f(ap):
            return ap.bitcast(F32)

        block = ctx.enter_context(nc.Block())

        @block.sync
        def _(sp):
            sp.dma_start(cb[:], cbook_b).then_inc(ld_cb, 16)
            sp.dma_start(pk[:], packed).then_inc(ld_const, 16)
            sp.dma_start(idraw[:], ids_b).then_inc(ld_const, 16)
            sp.dma_start(loraa_sb[:], loraa).then_inc(ld_const, 16)
            with sp.Fori(0, KC // 2) as t:
                for u in range(2):
                    rows = sp.snap(t * 256 + 128 * u)
                    sp.wait_ge(ws_lo[u], t + 1)
                    sp.dma_start(w_raw[u][:], chunked(w1[:, bass.ds(rows, P)])).then_inc(ld_w[u], 16)
                    sp.wait_ge(wd_ok[u], t + 1)
                    sp.dma_start(wq_sb[u][:], wq[bass.ds(rows, P), :]).then_inc(ld_q[u], 16)
                    sp.wait_ge(d_mm[u], t + 1)
                    sp.dma_start(lorab_sb[u][:], lorabt[:, bass.ds(rows, P)]).then_inc(ld_lorab[u], 16)
            for u in range(2):
                sp.wait_ge(ws_lo[u], KC // 2 + 1)
                sp.dma_start(w_raw[u][:], chunked(wbt[:, u * P:(u + 1) * P])).then_inc(ld_w[u], 16)
            for u in range(2):
                sp.wait_ge(we_lo[u], KC // 2 + 1)
            sp.dma_start(x0_raw[:], chunked(x0t)).then_inc(ld_rw0, 16)
            with sp.Fori(1, KC // 2) as t:
                for u in range(2):
                    cols_b = sp.snap(t * 256 + 128 * u)
                    sp.wait_ge(ws_lo[u], t + KC // 2 + 1)
                    sp.dma_start(w_raw[u][:], chunked(wbt[:, bass.ds(cols_b, P)])).then_inc(ld_w[u], 16)
            sp.wait_ge(x0_lo_s, 1)
            sp.dma_start(b0t_raw[:], chunked(b0t)).then_inc(ld_b0t, 16)
            sp.wait_ge(st_e, 32 * KC)
            sp.wait_ge(st_low, 16)
            sp.wait_ge(st_p1, 16)
            with sp.Fori(0, NB) as nb:
                col = sp.snap(nb * BW)
                for c in range(KC):
                    b = c % NR
                    sp.wait_ge(e_used[b], (nb * 2 + c // NR if b < KC - NR else nb) + 1)
                    if c < 2:
                        for u in range(2):
                            sp.wait_ge(b_mm[u], KC)
                        sp.wait_ge(mb_ok, KC)
                    sp.dma_start(e_raw[b][:], e_dram[c * P:(c + 1) * P, bass.ds(col, BW)]).then_inc(ld_e[b], 16)
            for b in range(NR):
                sp.wait_ge(e_used[b], (2 * NB if b < KC - NR else NB) + 1)
            for c in range(2):
                sp.dma_start(x_raw[c][:], xT[c * P:(c + 1) * P, 0:TT]).then_inc(ld_x[c], 16)
            sp.wait_ge(g_mm, (NB - 1) * KC + 1)
            for c in range(2, KC - 1):
                sp.dma_start(x_first[c][:], xT[c * P:(c + 1) * P, 0:TT]).then_inc(ld_xf[c - 2], 16)
            sp.wait_ge(xs_lo, 2)
            sp.dma_start(x_raw[1][:], xT[(KC - 1) * P:D, 0:TT]).then_inc(ld_x[1], 16)
            sp.wait_ge(xs_lo, KC - 1)
            sp.wait_ge(bias_mm, 1)
            sp.dma_start(p1_raw[:], p1_dram).then_inc(ld_p1, 16)
            sp.dma_start(lb1_raw[:], lb1).then_inc(ld_lb1, 16)

            def load_x(tile_cols, n, c):
                sp.wait_ge(xs_lo, n - 1)
                sp.dma_start(x_raw[c % 2][:], xT[c * P:(c + 1) * P, tile_cols]).then_inc(ld_x[c % 2], 16)

            with sp.Fori(1, NT) as tau:
                col = sp.snap(tau * TT)
                for c in range(KC):
                    load_x(bass.ds(col, TT), tau * KC + c, c)

        @block.gpsimd
        def _(pool):
            for c in range(KC):
                pool.dma_start(m1_raw[c][:], m1t[c * P:(c + 1) * P, :]).then_inc(ld_m1[c], 16)
            pool.dma_start(e_dram[:, LOW0:LOW0 + ER], aallt).then_inc(st_low, 16)
            pool.dma_start(bl1_raw[:], chunked(bl1)).then_inc(ld_bl, 16)
            with pool.Fori(0, KC) as k:
                pool.wait_ge(e_diag, k + 1)
                pool.dma_start(e_dram[bass.ds(k * P, P), 0:D], est[:, 0:D]).then_inc(st_e, 16)
                pool.dma_start(e_dram[bass.ds(k * P, P), MID0:NE], est[:, D:NM1]).then_inc(st_e, 16)
            pool.wait_ge(p1_ev, 3)
            pool.dma_start(p1_dram, est[:]).then_inc(st_p1, 16)
            pool.wait_ge(st_p1, 16)
            pool.dma_start(est[:], m1t[0:P, :]).then_inc(ld_mb[0], 16)
            for u in range(2):
                pool.wait_ge(d_mm[u], KC // 2 + 1)
            pool.dma_start(m1_again[1][:], m1t[P:2 * P, :]).then_inc(ld_mb[1], 16)
            with pool.Fori(1, KC // 2) as t:
                for u in range(2):
                    pool.wait_ge(mb_ok, t * 2 + u - 1)
                    pool.dma_start(m1_again[u][:], m1t[bass.ds((t * 2 + u) * P, P), :]).then_inc(ld_mb[u], 16)

        primed = {"pe": [*d_mm], "act": [*e_ev, *b_ev, lg_ok, *ev, rex_ok, *st_o],
                  "v": [*wd_ok, *weff_raw, *we_lo, *ws_lo, *e_used, *g_lo_s, v_lo, *c_lo, raw_ok]}

        @block.tensor
        def _(pe):
            for s in primed["pe"]:
                pe.sem_inc(s, 1)
            pe.sem_inc(eb_free, KC)

            def split_product(out_ap, lhs_hi, lhs_lo, rhs_hi, rhs_lo, first, last):
                nc.tensor.matmul(out_ap, lhs_hi, rhs_hi, start=first, stop=False)
                nc.tensor.matmul(out_ap, lhs_hi, rhs_lo, start=False, stop=False)
                return nc.tensor.matmul(out_ap, lhs_lo, rhs_hi, start=False, stop=last)

            pe.wait_ge(cols_ok, 1)
            nc.tensor.matmul(bk[7][0:LV, 0:1], tt_[0:1, 0:LV], one1[0:1, 0:1], start=True, stop=True)
            nc.tensor.matmul(bk[7][0:LV, 1:2], cb[0:1, :], one1[0:1, 0:1], start=True, stop=True)
            nc.tensor.matmul(bk[7][0:LV, 2:3], reach[0:1, :], one1[0:1, 0:1], start=True, stop=True).then_inc(cols_mm, 1)
            pe.wait_ge(cols_ok, 2)
            nc.tensor.matmul(bk[7][0:LV, 3:4], tri, cols[:, 2:3], start=True, stop=True).then_inc(rank_mm, 1)
            pe.wait_ge(sel_ok, 1)
            for i in range(3):
                mm = nc.tensor.matmul(bk[7][:, 64 + 64 * i:128 + 64 * i], cols[:, i:i + 1].to_broadcast([LV, P]),
                                      selm[:], start=True, stop=True)
            mm.then_inc(comp_mm, 1)

            pe.wait_ge(ld_const, 16 * N_CONST)

            def delta(t, u):
                pe.wait_ge(ld_lorab[u], t * 16 + 16)
                pe.wait_ge(weff_raw[u], t + 1)
                for h in range(2):
                    mm = nc.tensor.matmul(bk[2 * u + h][:], lorab_sb[u][:], loraa_sb[:, h * 512:(h + 1) * 512],
                                          start=True, stop=True)
                mm.then_inc(d_mm[u], 1)

            def e_rows(t, u):
                pe.wait_ge(ws_hi[u], t + 1)
                pe.wait_ge(ws_lo[u], t + 1 + 1)
                for g, (n0, n) in enumerate(A_COLS):
                    pe.wait_ge(e_ev[g], t * 2 + u + 1)
                    for c in range(KC):
                        mm = split_product(bk[4 + g][:, 0:n], w_hi[u][:, c, :], w_lo[u][:, c, :],
                                           m1_hi[:, c, n0:n0 + n], m1_lo[:, c, n0:n0 + n], c == 0, c == KC - 1)
                    mm.then_inc(e_mm[u], 1)

            delta(0, 0)
            delta(0, 1)
            pe.wait_ge(ws_hi[0], 1)
            pe.wait_ge(ws_lo[0], 1 + 1)
            for c in range(KC):
                pe.wait_ge(m1_hi_s, c + 1)
                pe.wait_ge(m1_lo_s, c + 1)
                for g, (n0, n) in enumerate(A_COLS):
                    mm = split_product(bk[4 + g][:, 0:n], w_hi[0][:, c, :], w_lo[0][:, c, :],
                                       m1_hi[:, c, n0:n0 + n], m1_lo[:, c, n0:n0 + n], c == 0, c == KC - 1)
                    if c == KC - 1:
                        mm.then_inc(e_mm[0], 1)
            e_rows(0, 1)
            with pe.Fori(1, KC // 2) as t:
                delta(t, 0)
                delta(t, 1)
                e_rows(t, 0)
                e_rows(t, 1)
            for u in range(2):
                pe.wait_ge(ws_hi[u], 1 + KC // 2)
                pe.wait_ge(ws_lo[u], 1 + KC // 2 + 1)
                for c in range(KC):
                    if u == 0:
                        pe.wait_ge(we_hi[c % 2], c // 2 + 1)
                        pe.wait_ge(we_lo[c % 2], c // 2 + 1 + 1)
                    for h in range(2):
                        g = B0_BANKS[2 * u + h]
                        if c == 0 and g < 3:
                            pe.wait_ge(e_ev[g], KC + 1)
                        mm = split_product(bk[4 + g][:], w_hi[u][:, c, :], w_lo[u][:, c, :],
                                           weff_hi[:, c, h * 512:(h + 1) * 512], weff_lo[:, c, h * 512:(h + 1) * 512],
                                           c == 0, c == KC - 1)
                        if c == KC - 1:
                            mm.then_inc(b_mm[u], 1)
            pe.wait_ge(bl_hi, 1)
            pe.wait_ge(bl_lo, 1)
            for u in range(2):
                pe.wait_ge(weff_raw[u], KC // 2 + 1)
            for g, (n0, n) in enumerate(A_COLS):
                for c in range(KC):
                    mm = split_product(bk[1 + g][:, 0:n], bl1_hi[:, c, :], bl1_lo[:, c, :],
                                       m1_hi[:, c, n0:n0 + n], m1_lo[:, c, n0:n0 + n], c == 0, c == KC - 1)
                mm.then_inc(p1_mm, 1)
            with pe.Fori(1, KC // 2) as t:
                for u in range(2):
                    pe.wait_ge(ws_hi[u], t + 1 + KC // 2)
                    pe.wait_ge(ws_lo[u], t + 1 + KC // 2 + 1)
                    for h in range(2):
                        pe.wait_ge(b_ev[u], t * 2 + h - 1)
                        if 2 * u + h:
                            pe.wait_ge(p1_ev, 2 * u + h)
                        for c in range(KC):
                            mm = split_product(bk[2 * u + h][:], w_hi[u][:, c, :], w_lo[u][:, c, :],
                                               weff_hi[:, c, h * 512:(h + 1) * 512], weff_lo[:, c, h * 512:(h + 1) * 512],
                                               c == 0, c == KC - 1)
                        mm.then_inc(b_mm[u], 1)
            pe.wait_ge(x0_hi_s, 1)
            pe.wait_ge(x0_lo_s, 1)
            for i in range(KC):
                if i < 4:
                    pe.wait_ge(b_ev[i // 2], 3)
                else:
                    pe.wait_ge(h_sum, i - 3)
                for c in range(KC):
                    for k, w in enumerate((weff_hi, weff_lo)):
                        mm = nc.tensor.matmul(bk[4 + i % 4][:, 0:2 * NX0], w[:, c, i * P:(i + 1) * P], x0_hl[:, c, :],
                                              start=c + k == 0, stop=c + k == KC)
                mm.then_inc(h_mm, 1)
            for u in range(2):
                pe.wait_ge(c_hi[u], KC // 2)
                pe.wait_ge(c_lo[u], KC // 2 + 1)
            pe.wait_ge(b0t_hi_s, 1)
            pe.wait_ge(b0t_lo_s, 1)
            with pe.Fori(0, NB) as nb:
                for r in range(KC + 1):
                    b = r % 3
                    pe.wait_ge(g_lo_s[b], nb * 3 + r // 3 + 1)
                    for c in range(KC):
                        if r == 0:
                            pe.wait_ge(eb_hi_s, nb * KC + c + 1)
                            pe.wait_ge(eb_lo_s, nb * KC + c + 1)
                        cs = slice((r - 1) * P, r * P)
                        lh, ll = (c0_hi[:, c, cs], c0_lo[:, c, cs]) if r else (b0t_hi[:, c, :], b0t_lo[:, c, :])
                        mm = split_product(bk[b][:, 0:BW], lh, ll, eb_hi[:, c, :], eb_lo[:, c, :], c == 0, c == KC - 1)
                        if r == KC:
                            mm.then_inc(eb_free, 1)
                    if r < KC:
                        mm.then_inc(g_mm, 1)
            for b in range(NR):
                pe.wait_ge(e_used[b], (2 * NB if b < KC - NR else NB) + 1)
            pe.wait_ge(b_ev[1], 3)
            for m in range(10):
                nc.tensor.matmul(bk[7][:, m:m + 1], bacc[:, m * P:(m + 1) * P], ones[:, 0:1], start=True, stop=True)
            nc.tensor.matmul(bk[7][0:E, 10:11], bacc[:, LG0:NE], ones[:, 0:1], start=True, stop=True).then_inc(bias_mm, 1)

            L, H, LOW, MID, TR = bk[0], bk[1], bk[2], bk[3], bk[4]
            OUT = [bk[5], bk[6], bk[7], H, LOW, bk[5], bk[6], bk[7]]

            def tile(t, u):
                tau = t * 2 + u

                def from_x(out_ap, hi, lo, n0, n, last=False, l0=None):
                    l0 = n0 if l0 is None else l0
                    for c in range(KC):
                        mm = split_product(out_ap, hi[:, c, n0:n0 + n], lo[:, c, l0:l0 + n],
                                           x_hi[u][:, c, :], x_lo[u][:, c, :], c == 0, last and c == KC - 1)
                    return mm

                def from_v(out_ap, v, hi, lo, n0, n, last=False):
                    return split_product(out_ap, hi[:, n0:n0 + n], lo[:, n0:n0 + n], mv_hi[v][:], mv_lo[v][:],
                                         False, last)

                def turn(k, rows):
                    pe.wait_ge(lg_ok, tau * 2 + k + 1 + 1)
                    for s in range(4):
                        mm = nc.tensor.matmul(TR[:, E * s:E * s + E], lg_sb[0:rows, s * P:(s + 1) * P],
                                              sel[k], start=True, stop=True)
                    mm.then_inc(lgt_mm, 1)

                def to_logit1(v, lg, last):
                    nc.tensor.matmul(L[0:2 * E, :], lg, mv_hi[v][:], start=False, stop=False, skip_group_check=True)
                    return nc.tensor.matmul(L[0:2 * E, :], lg, mv_lo[v][:], start=False, stop=last,
                                            skip_group_check=True)

                def spread(k):
                    pe.wait_ge(w_ok, tau * 2 + k + 1)
                    for s in range(4):
                        mm = nc.tensor.transpose(TR[:, s * P:(s + 1) * P], wrep[:, s * P:(s + 1) * P], ident)
                    mm.then_inc(wx_mm, 1)

                pe.wait_ge(lg_ok, tau * 2 + 1)
                for c in range(KC):
                    pe.wait_ge(xs_hi, tau * KC + c + 1)
                    pe.wait_ge(xs_lo, tau * KC + c + 1)
                    for k, x in enumerate((x_hi[u], x_lo[u])):
                        mm = nc.tensor.matmul(L[0:NGL, :], gx[:, c, 0:NGL], x[:, c, :], start=c + k == 0,
                                              stop=c + k == KC)
                mm.then_inc(lx_mm, 1)
                pe.wait_ge(ev[1], tau * 4 + 1)
                from_x(H[:], gx, h0_lo, NGL, ER, True, 0).then_inc(h0_mm, 1)
                pe.wait_ge(ev[0], tau * 4 + 1)
                from_x(LOW[:], g_hi, g_lo, LOW0, ER)
                turn(0, NGL)
                pe.wait_ge(v_lo, tau * 3 + 1)
                from_x(MID[:], g_hi, g_lo, MID0, ER)
                from_x(OUT[0][:], g_hi, g_lo, 0, P)
                spread(0)
                from_x(OUT[1][:], g_hi, g_lo, P, P)
                pe.wait_ge(v_hi, tau * 3 + 1)
                pe.wait_ge(v_lo, tau * 3 + 1 + 1)
                pe.wait_ge(f_hi, 2)
                pe.wait_ge(f_lo, 2)
                from_v(LOW[:], "m0", p0_hi, p0_lo, LOW0, ER, True).then_inc(low_mm, 1)
                from_v(MID[:], "m0", p0_hi, p0_lo, MID0, ER)
                to_logit1("m0", p0_lg, False)
                from_x(OUT[2][:], g_hi, g_lo, 2 * P, P)
                pe.wait_ge(v_hi, tau * 3 + 2)
                pe.wait_ge(v_lo, tau * 3 + 2 + 1)
                to_logit1("low", p1_lg, True).then_inc(lg1_mm, 1)
                from_v(MID[:], "low", p1_hi, p1_lo, D, ER, True).then_inc(mid_mm, 1)
                for m in range(3):
                    from_v(OUT[m][:], "m0", p0_hi, p0_lo, m * P, P)
                turn(1, 2 * E)
                for m in range(3):
                    from_v(OUT[m][:], "low", p1_hi, p1_lo, m * P, P)
                for m in (3, 4):
                    if m == 4:
                        spread(1)
                    from_x(OUT[m][:], g_hi, g_lo, m * P, P)
                    from_v(OUT[m][:], "m0", p0_hi, p0_lo, m * P, P)
                    from_v(OUT[m][:], "low", p1_hi, p1_lo, m * P, P)
                pe.wait_ge(v_hi, tau * 3 + 3)
                pe.wait_ge(v_lo, tau * 3 + 3 + 1)
                for m in range(KC):
                    if m >= 5:
                        pe.wait_ge(ev[(m - 5) % 2], tau * 4 + (m - 5) // 2 + 1 + 1)
                        from_x(OUT[m][:], g_hi, g_lo, m * P, P)
                        from_v(OUT[m][:], "m0", p0_hi, p0_lo, m * P, P)
                        from_v(OUT[m][:], "low", p1_hi, p1_lo, m * P, P)
                    from_v(OUT[m][:], "mid", lb1_hi, lb1_lo, m * P, P, True).then_inc(out_mm, 1)

            pe.wait_ge(bias_ok, 1)
            for b in range(3):
                pe.wait_ge(g_lo_s[b], NB * 3 + 1)
            pe.wait_ge(h_lo, KC)
            with pe.Fori(0, NT // 2) as t:
                for u in range(2):
                    tile(t, u)

        @block.scalar
        def _(act):
            for s in primed["act"]:
                act.sem_inc(s, 1)

            def hi_of(dst, src):
                return nc.scalar.activation(dst, src, ACT.Identity)

            def w_split(t, u, used, per, done):
                act.wait_ge(ld_w[u], t * 16 + 16 + 16 * done)
                if used is not None:
                    act.wait_ge(used[u], t * per)
                hi_of(w_hi[u][:], w_raw[u][:]).then_inc(ws_hi[u], 1)

            def e_out(t, u, groups=range(3)):
                for g in groups:
                    if g == 0 and (not isinstance(t, int) or 2 * t + u):
                        act.wait_ge(st_e, (t * 2 + u) * 32)
                    n0, n = A_COLS[g]
                    act.wait_ge(e_mm[u], t * 3 + g + 1)
                    nc.scalar.activation(est[:, n0:n0 + n], bk[4 + g][:, 0:n], ACT.Identity).then_inc(e_ev[g], 1)

            def quant_pair(t, first):
                if not first:
                    e_out(t - 1, 1)
                    w_split(t, 1, e_mm, 3, 0)
                for u in range(2):
                    act.wait_ge(wd_ok[u], t + 1 + 1)
                    if first:
                        act.wait_ge(rs_ok, 1)
                    for g in range(VS_ACT if u else KC):
                        gs = qbuf[u][:, g * GRP:(g + 1) * GRP]
                        ins = nc.scalar.activation(gs, gs, ACT.Identity, scale=rscale[:, bass.ds(t * 16 + 8 * u + g, 1)])
                    ins.then_inc(q_ok[u], 1)
                for m in range(NF - 1, 0, -1):
                    for u in range(2):
                        act.wait_ge(r_ready[u], t * NF + NF - m)
                        nc.scalar.activation(rbuf[u][:], rbuf[u][:], ACT.Identity, bias=step[:, m:m + 1]).then_inc(a_ready[u], 1)
                    g = E_OUT_AT[first].get(m)
                    if g is not None:
                        e_out(t, 0, [g])
                act.wait_ge(r_ready[0], t * NF + NF)
                for g in range(VS_ACT):
                    gs, k = rbuf[0][:, g * GRP:(g + 1) * GRP], bass.ds(t * 16 + g, 1)
                    ins = nc.scalar.activation(gs, gs, ACT.Identity, bias=vscale[:, k], scale=scale[:, k])
                ins.then_inc(vs_ok, 1)
                w_split(t + 1, 0, e_mm, 3, 0)
                for u in range(2):
                    act.wait_ge(weff_raw[u], t + 1 + 1)
                    if first:
                        act.wait_ge(m1_lo_s, KC)
                    hi_of(weff_hi[:, bass.ds(t * 2 + u, 1), :].squeeze(1), qbuf[u][:]).then_inc(we_hi[u], 1)

            w_split(0, 0, None, 0, 0)
            for c in range(KC):
                act.wait_ge(ld_m1[c], 16)
                hi_of(m1_hi[:, c, :], m1_raw[c][:]).then_inc(m1_hi_s, 1)
                if c == 4:
                    w_split(0, 1, None, 0, 0)
            quant_pair(0, True)
            with act.Fori(1, KC // 2) as t:
                quant_pair(t, False)
            e_out(KC // 2 - 1, 1)
            w_split(KC // 2, 1, e_mm, 3, 0)
            act.wait_ge(ld_bl, 16)
            for u in range(2):
                act.wait_ge(wd_ok[u], KC // 2 + 1)
            hi_of(bl1_hi[:], bl1_raw[:]).then_inc(bl_hi, 1)

            def c0_out(t, u, banks=range(4)):
                for h in range(2):
                    act.wait_ge(b_mm[u], t * 2 + h + 1)
                    act.wait_ge(c_lo[u], t + 1)
                    nc.scalar.activation(tmp[u][:, h * 512:(h + 1) * 512], bk[banks[2 * u + h]][:], ACT.Identity).then_inc(b_ev[u], 1)
                act.wait_ge(b_diag[u], t + 1)
                hi_of(c0_hi[:, bass.ds(t * 2 + u, 1), :].squeeze(1), tmp[u][:]).then_inc(c_hi[u], 1)

            for u in range(2):
                w_split(1, u, b_mm, 2, KC // 2)
            act.wait_ge(ld_rw0, 16)
            hi_of(x0_hl[:, :, 0:NX0], x0_raw[:]).then_inc(x0_hi_s, 1)
            act.wait_ge(st_e, 32 * KC)
            for g, (n0, n) in enumerate(A_COLS):
                act.wait_ge(p1_mm, g + 1)
                nc.scalar.activation(est[:, n0:n0 + n], bk[1 + g][:, 0:n], ACT.Identity).then_inc(p1_ev, 1)
            for u in range(2):
                c0_out(0, u, [4 + g for g in B0_BANKS])
            with act.Fori(1, KC // 2 - 1) as t:
                for u in range(2):
                    c0_out(t, u)
                    w_split(t + 1, u, b_mm, 2, KC // 2)
            c0_out(KC // 2 - 1, 0)
            act.wait_ge(ld_b0t, 16)
            act.wait_ge(mb_ok, KC - 1)
            hi_of(b0t_hi[:], b0t_raw[:]).then_inc(b0t_hi_s, 1)
            c0_out(KC // 2 - 1, 1)

            def e_split(nb, c):
                b = c % NR
                act.wait_ge(ld_e[b], (nb * 32 + 16 * (c // NR) if b < KC - NR else nb * 16) + 16)
                act.wait_ge(eb_free, nb * KC + c + 1)
                hi_of(eb_hi[:, c, :], e_raw[b][:]).then_inc(eb_hi_s, 1)

            def h_copy(i):
                act.wait_ge(h_mm, i + 1)
                if i >= 2:
                    act.wait_ge(h_lo, i - 1)
                nc.scalar.activation(hx[i % 2][:], bk[4 + i % 4][:, 0:NX0], ACT.Identity).then_inc(h_cp, 1)

            h_copy(0)
            for i in range(KC):
                if i + 1 < KC:
                    h_copy(i + 1)
                act.wait_ge(h_sum, i + 1)
                hi_of(gx[:, i, 3 * E:NGL + ER], hx[i % 2][:]).then_inc(h_hi, 1)
                e_split(0, i)

            def g_out(nb, r, last):
                if r == KC:
                    act.wait_ge(eb_free, nb * KC + 2 * KC)
                else:
                    act.wait_ge(g_mm, nb * KC + r + 1)
                src, i = bk[r % 3], r - 1
                if r == 0:
                    hi_of(p0_hi[:, bass.ds(nb * BW, BW)], src[:, 0:BW]).then_inc(g_hi_s, 1)
                elif last:
                    w = GM - nb * BW
                    hi_of(g_hi[:, i, nb * BW:GM], src[:, 0:w])
                    hi_of(gx[:, i, 0:E], src[:, w:BW]).then_inc(g_hi_s, 1)
                else:
                    hi_of(g_hi[:, i, bass.ds(nb * BW, BW)], src[:, 0:BW]).then_inc(g_hi_s, 1)

            with act.Fori(0, NB - 1) as nb:
                for r in range(KC):
                    g_out(nb, r, False)
                for c in range(KC):
                    e_split(nb + 1, c)
                g_out(nb, KC, False)
            for r in range(KC + 1):
                g_out(NB - 1, r, True)

            def x_split(n, u, c):
                act.wait_ge(ld_x[c % 2], n * 64 + 16 * (c // 2) + 16 - (48 if c % 2 == 0 else 32))
                hi_of(x_hi[u][:, c, :], x_raw[c % 2][:]).then_inc(xs_hi, 1)

            for c in range(KC):
                if c < 2:
                    act.wait_ge(ld_x[c], 16)
                elif c < KC - 1:
                    act.wait_ge(ld_xf[c - 2], 16)
                else:
                    act.wait_ge(ld_x[1], 32)
                hi_of(x_hi[0][:, c, :], x_first[c][:]).then_inc(xs_hi, 1)
            act.wait_ge(bias_ok, 1)
            act.wait_ge(ld_p1, 16)
            hi_of(p1_hi, p1_raw[:]).then_inc(f_hi, 1)
            act.wait_ge(ld_lb1, 16)
            hi_of(lb1_hi[:], lb1_raw[:]).then_inc(f_hi, 1)
            act.wait_ge(f_lo, 2)

            L, TR, H, LOW = bk[0], bk[4], bk[1], bk[2]
            OUT = [bk[5], bk[6], bk[7], H, LOW, bk[5], bk[6], bk[7]]

            def store(t, u, m):
                act.wait_ge(ev[m % 2], (t * 2 + u) * 4 + m // 2 + 1 + 1)
                act.dma_start(out[m * P:(m + 1) * P, bass.ds((t * 2 + u) * TT, TT)],
                              ost[m % 2][:]).then_inc(st_o[m % 2], 16)

            def tile(t, u, more):
                tau = t * 2 + u

                def routed(k):
                    act.wait_ge(dif_ok, tau * 2 + k + 1)
                    nc.scalar.activation(rs4[2][:], rs4[2][:], ACT.Exp).then_inc(rex_ok, 1)
                    act.wait_ge(wx_mm, tau * 2 + k + 1)
                    nc.scalar.activation(wx_sb[:], TR[:], ACT.Identity).then_inc(wx_ok, 1)

                def v_split(k, v):
                    act.wait_ge(raw_ok, tau * 3 + k + 1 + 1)
                    hi_of(mv_hi[v][:], mraw[:]).then_inc(v_hi, 1)

                act.wait_ge(lx_mm, tau + 1)
                act.wait_ge(raw_ok, tau * 3 + 1)
                nc.scalar.activation(lg_sb[:], L[0:NGL, :], ACT.Identity).then_inc(lg_ok, 1)
                routed(0)
                v_split(0, "m0")
                v_split(1, "low")
                act.wait_ge(lg1_mm, tau + 1)
                nc.scalar.activation(lg_sb[0:2 * E, :], L[0:2 * E, :], ACT.Identity, bias=biasv[0:2 * E, 10:11]).then_inc(lg_ok, 1)
                routed(1)
                v_split(2, "mid")
                for m in range(KC):
                    if more:
                        x_split(tau + 1, 1 - u, m)
                    act.wait_ge(out_mm, tau * KC + m + 1)
                    act.wait_ge(st_o[m % 2], (tau * 4 + m // 2) * 16 + 1)
                    nc.scalar.activation(ost[m % 2][:], OUT[m][:], ACT.Identity,
                                         bias=biasv[:, m:m + 1]).then_inc(ev[m % 2], 1)
                    if m:
                        store(t, u, m - 1)
                store(t, u, KC - 1)

            with act.Fori(0, NT // 2 - 1) as t:
                tile(t, 0, True)
                tile(t, 1, True)
            tile(NT // 2 - 1, 0, True)
            tile(NT // 2 - 1, 1, False)
            for b in range(2):
                act.wait_ge(st_o[b], 16 * NT * KC // 2 + 1)

        @block.vector
        def _(v):
            for s in primed["v"]:
                v.sem_inc(s, 1)

            count = [0]

            def link(ins, at_=None):
                ins.then_inc(dve, 1)
                count[0] += 1
                v.wait_ge(dve, count[0] if at_ is None else at_ + count[0])

            def lo_of(dst, src, hi):
                return nc.vector.tensor_tensor(dst, src, f(hi), ALU.subtract)

            def w_split(t, u, done=0):
                v.wait_ge(ws_hi[u], t + 1 + done)
                lo_of(w_lo[u][:], w_raw[u][:], w_hi[u][:]).then_inc(ws_lo[u], 1)

            def m1_split(c):
                v.wait_ge(m1_hi_s, c + 1)
                lo_of(m1_lo[:, c, :], m1_raw[c][:], m1_hi[:, c, :]).then_inc(m1_lo_s, 1)

            def scale_step(k):
                magic = 12582912.0
                ts, stt = nc.vector.tensor_scalar, nc.vector.scalar_tensor_tensor
                if k == 0:
                    return ts(ex_r[:], slog, -87.0, 88.0, ALU.max, ALU.min)
                if k == 1:
                    return ts(ex_n[:], ex_r[:], 1.4426950408889634, magic, ALU.mult, ALU.add)
                if k == 2:
                    return ts(ex_n[:], ex_n[:], magic, None, ALU.subtract)
                if k in (3, 4):
                    part = -0.693359375 if k == 3 else 2.12194440054690583e-4
                    return stt(ex_r[:], ex_n[:], part, ex_r[:], ALU.mult, ALU.add)
                if k == 5:
                    return ts(ex_p[:], ex_r[:], 1.0 / 5040, None, ALU.mult)
                if k < 12:
                    return stt(ex_p[:], ex_p[:], 1.0 / (720, 120, 24, 6, 2, 1)[k - 6], ex_r[:], ALU.add, ALU.mult)
                if k == 12:
                    return ts(ex_i[:], ex_n[:], 127.0, 8388608.0, ALU.add, ALU.mult)
                if k == 13:
                    return stt(scale[:], ex_p[:], 1.0, ex_i[:].bitcast(F32), ALU.add, ALU.mult)
                return nc.vector.reciprocal(rscale[:], scale[:])

            nc.vector.memset(ones[:], 1.0)
            nc.vector.memset(one1[:], 1.0)
            nc.vector.memset(tt_[:, 0:1], -4.0)
            nc.vector.memset(biasv[:], 0.0)
            link(nc.vector.memset(tt_[:, LV:LV + 1], 4.0))
            v.wait_ge(ld_cb, 16)
            link(nc.vector.tensor_scalar(vcomp[:], cb[:], -1.0, None, ALU.mult))
            link(nc.vector.tensor_tensor(vcomp[:], vcomp[:], cb[:], ALU.max))
            link(nc.vector.reduce_max(val0[:], vcomp[:], AX_X))
            link(nc.vector.tensor_scalar(val0[:], val0[:], 1e-8, None, ALU.max))
            link(nc.vector.reciprocal(val0[:], val0[:]))
            link(nc.vector.tensor_scalar(cb[:], cb[:], val0[:, 0:1], None, ALU.mult))
            v.wait_ge(ld_const, 16 * N_CONST)
            nc.vector.tensor_tensor(tt_[:, 1:LV], cb[:, 0:LV - 1], cb[:, 1:LV], ALU.add)
            link(scale_step(0))
            nc.vector.tensor_scalar(tt_[:, 1:LV], tt_[:, 1:LV], 0.5, None, ALU.mult)
            link(scale_step(1))
            for h in range(1, 6):
                half = 1 << h
                view = tt_[:, 0:LV].rearrange("p (b w) -> p b w", w=2 * half)
                mid = view[:, :, half:half + 1].to_broadcast([P, LV // (2 * half), half - 1])
                nc.vector.tensor_tensor(view[:, :, 1:half], view[:, :, 1:half], mid, ALU.min)
                link(scale_step(2 * h))
                nc.vector.tensor_tensor(view[:, :, half + 1:2 * half], view[:, :, half + 1:2 * half], mid, ALU.max)
                link(scale_step(2 * h + 1))
            nc.vector.tensor_tensor(reach[:], tt_[:, 0:LV], tt_[:, 1:LV + 1], ALU.is_lt)
            link(scale_step(12))
            nc.vector.reduce_sum(rs4[0][:, 0:1], reach[:], AX_X)
            link(scale_step(13))
            nc.vector.tensor_copy(cnt[:, 0:1], rs4[0][:, 0:1]).then_inc(cols_ok, 1)
            w_split(0, 0)
            v.wait_ge(cols_mm, 1)
            nc.vector.tensor_copy(cols[:, 0:3], bk[7][0:LV, 0:3]).then_inc(cols_ok, 1)
            v.wait_ge(rank_mm, 1)
            link(nc.vector.tensor_copy(cols[:, 3:4], bk[7][0:LV, 3:4]))
            nc.vector.tensor_scalar(selm[:], iota, cols[:, 3:4], cols[:, 2:3], ALU.is_equal, ALU.mult).then_inc(sel_ok, 1)
            m1_split(0)
            v.wait_ge(comp_mm, 1)
            nc.vector.tensor_copy(thr[:], bk[7][:, 64:128])
            nc.vector.tensor_copy(vcomp[:], bk[7][:, 128:192])
            link(nc.vector.tensor_copy(valid[:], bk[7][:, 192:256]))
            nc.vector.tensor_copy(val0[:], vcomp[:, 0:1])
            nc.vector.tensor_copy(step[:, 0:1], vcomp[:, 0:1])
            link(nc.vector.tensor_tensor(step[:, 1:LV], vcomp[:, 1:LV], vcomp[:, 0:LV - 1], ALU.subtract))
            link(nc.vector.tensor_tensor(step[:, 1:LV], step[:, 1:LV], valid[:, 1:LV], ALU.mult))
            nc.vector.tensor_scalar(vscale[:], scale[:], val0[:, 0:1], None, ALU.mult)
            scale_step(14).then_inc(rs_ok, 1)
            link(nc.vector.tensor_copy(idf[:], idraw[:]))
            link(nc.vector.tensor_scalar(mask_s[:], idf[:], nidx, sfc, ALU.is_equal, ALU.mult))
            leaves = v.value_load(cnt[0:1, 0:1], min_val=0, max_val=LV)

            def add_identity(dst, t, u, s):
                sl = dst[:, bass.ds((t * 2 + u) * P, P)]
                nc.vector.tensor_tensor(sl, sl, ident, ALU.add).then_inc(s, 1)

            def e_diagonal(t, u):
                for g in range(3):
                    v.wait_ge(e_ev[g], t * 2 + u + 1 + 1)
                add_identity(est, t, u, e_diag)

            halves = [(bk[2 * u], bk[2 * u + 1]) for u in range(2)]

            def weff_low(t, u):
                v.wait_ge(weff_raw[u], t + 1 + 1)
                v.wait_ge(we_hi[u], t + 1)
                k = bass.ds(t * 2 + u, 1)
                lo_of(weff_lo[:, k, :].squeeze(1), qbuf[u][:], weff_hi[:, k, :].squeeze(1)).then_inc(we_lo[u], 1)

            def dequant_input(t, u):
                v.wait_ge(d_mm[u], t + 1 + 1)
                v.wait_ge(ld_q[u], t * 16 + 16)
                if not isinstance(t, int):
                    v.wait_ge(we_lo[u], t + 1)
                for h in range(2):
                    cs = slice(h * 512, (h + 1) * 512)
                    ins = nc.vector.scalar_tensor_tensor(qbuf[u][:, cs], halves[u][h][:], 0.5, wq_sb[u][:, cs],
                                                         ALU.mult, ALU.add)
                ins.then_inc(wd_ok[u], 1)

            def quant_pair(t, first, at_):
                c0 = count[0]
                for u in range(2):
                    if not first:
                        weff_low(t - 1, u)
                    dequant_input(t, u)
                    if u == 0 and not first:
                        e_diagonal(t - 1, 1)
                if first:
                    for c in range(4, KC):
                        m1_split(c)
                    w_split(0, 1)
                else:
                    w_split(t, 1)
                v.wait_ge(wd_ok[1], t + 1 + 1)
                sc = rscale[:, bass.ds(t * 16 + 8 + VS_ACT, KC - VS_ACT)].unsqueeze(2).to_broadcast([P, KC - VS_ACT, GRP])
                q3 = qbuf[1][:].rearrange("p (g w) -> p g w", w=GRP)[:, VS_ACT:KC, :]
                nc.vector.tensor_tensor(q3, q3, sc, ALU.mult).then_inc(q_tail, 1)
                with v.If(leaves > NF + 1):
                    v.wait_ge(q_tail, t + 1)
                    for u in range(2):
                        v.wait_ge(q_ok[u], t + 1)
                        nc.vector.memset(rbuf[u][:], 0.0)
                    with v.Fori(0, LV - 1 - NF) as j:
                        for u in range(2):
                            v.drain()
                            nc.vector.tensor_scalar(rbuf[u][:], rbuf[u][:], step[:, bass.ds(j * -1 + LV - 1, 1)], None, ALU.add)
                            v.drain()
                            nc.vector.scalar_tensor_tensor(rbuf[u][:], qbuf[u][:], thr[:, bass.ds(j * -1 + LV - 1, 1)],
                                                           rbuf[u][:], ALU.is_gt, ALU.mult)
                    v.drain()
                    for u in range(2):
                        nc.vector.tensor_scalar(rbuf[u][:], rbuf[u][:], step[:, NF:NF + 1], None, ALU.add)
                    v.drain()
                    for u in range(2):
                        nc.vector.scalar_tensor_tensor(rbuf[u][:], qbuf[u][:], thr[:, NF:NF + 1], rbuf[u][:],
                                                       ALU.is_gt, ALU.mult).then_inc(r_ready[u], 1)
                with v.Else():
                    v.wait_ge(q_tail, t + 1)
                    for u in range(2):
                        v.wait_ge(q_ok[u], t + 1)
                        nc.vector.tensor_scalar(rbuf[u][:], qbuf[u][:], thr[:, NF:NF + 1], step[:, NF:NF + 1],
                                                ALU.is_gt, ALU.mult).then_inc(r_ready[u], 1)
                for m in range(NF - 1, 0, -1):
                    for u in range(2):
                        v.wait_ge(a_ready[u], t * (NF - 1) + NF - m)
                        nc.vector.scalar_tensor_tensor(rbuf[u][:], qbuf[u][:], thr[:, m:m + 1], rbuf[u][:],
                                                       ALU.is_gt, ALU.mult).then_inc(r_ready[u], 1)
                    if m == (2 if first else 1):
                        e_diagonal(t, 0)
                v.wait_ge(r_ready[1], t * NF + NF)
                for u, g0 in ((1, 0), (0, VS_ACT)):
                    r3 = rbuf[u][:].rearrange("p (g w) -> p g w", w=GRP)[:, g0:KC, :]
                    sc = scale[:, bass.ds(t * 16 + 8 * u + g0, KC - g0)].unsqueeze(2).to_broadcast([P, KC - g0, GRP])
                    ins = nc.vector.scalar_tensor_tensor(r3, r3, val0[:, 0:1], sc, ALU.add, ALU.mult)
                link(ins, at_)
                for u in range(2):
                    if u == 0:
                        v.wait_ge(vs_ok, t + 1)
                    for h in range(2):
                        cs = slice(h * 512, (h + 1) * 512)
                        ins = nc.vector.scalar_tensor_tensor(qbuf[u][:, cs], halves[u][h][:], 0.5, rbuf[u][:, cs],
                                                             ALU.mult, ALU.add)
                    ins.then_inc(weff_raw[u], 1)
                w_split(t + 1, 0)
                return count[0] - c0

            for c in range(1, 4):
                m1_split(c)
            per = quant_pair(0, True, None)
            after = count[0]
            with v.Fori(1, KC // 2) as t:
                quant_pair(t, False, (t - 1) * per)
            count[0] = after + per * (KC // 2 - 1)
            for u in range(2):
                weff_low(KC // 2 - 1, u)
            e_diagonal(KC // 2 - 1, 1)
            w_split(KC // 2, 1)
            v.wait_ge(bl_hi, 1)
            lo_of(bl1_lo[:], bl1_raw[:], bl1_hi[:]).then_inc(bl_lo, 1)

            def c0_out(t, u):
                v.wait_ge(b_ev[u], t * 2 + 2 + 1)
                add_identity(tmp[u], t, u, b_diag[u])
                v.wait_ge(b_diag[u], t + 1)
                v.wait_ge(c_hi[u], t + 1)
                k = bass.ds(t * 2 + u, 1)
                lo_of(c0_lo[:, k, :].squeeze(1), tmp[u][:], c0_hi[:, k, :].squeeze(1)).then_inc(c_lo[u], 1)

            def m1_bias(t, u):
                if not isinstance(t, int) or 2 * t + u:
                    v.wait_ge(mb_ok, t * 2 + u)
                v.wait_ge(ld_mb[u], t * 16 + 16)
                b, m = b1c[:, bass.ds(t * 2 + u, 1)], m1_again[u]
                nc.vector.scalar_tensor_tensor(bacc[:, 0:D], m[:, 0:D], b, bacc[:, 0:D], ALU.mult, ALU.add)
                nc.vector.scalar_tensor_tensor(bacc[:, MID0:NE], m[:, D:NM1], b, bacc[:, MID0:NE],
                                               ALU.mult, ALU.add).then_inc(mb_ok, 1)

            for u in range(2):
                w_split(1, u, KC // 2)
            v.wait_ge(x0_hi_s, 1)
            lo_of(x0_hl[:, :, NX0:2 * NX0], x0_raw[:], x0_hl[:, :, 0:NX0]).then_inc(x0_lo_s, 1)
            v.wait_ge(p1_mm, 3)
            nc.vector.memset(bacc[:], 0.0).then_inc(bacc0, 1)
            for u in range(2):
                c0_out(0, u)
            v.wait_ge(bacc0, 1)
            for u in range(2):
                m1_bias(0, u)
            with v.Fori(1, KC // 2 - 1) as t:
                for u in range(2):
                    c0_out(t, u)
                    w_split(t + 1, u, KC // 2)
                    m1_bias(t, u)
            c0_out(KC // 2 - 1, 0)
            for u in range(2):
                m1_bias(KC // 2 - 1, u)
            v.wait_ge(b0t_hi_s, 1)
            lo_of(b0t_lo[:], b0t_raw[:], b0t_hi[:]).then_inc(b0t_lo_s, 1)
            c0_out(KC // 2 - 1, 1)

            def e_split(nb, c):
                v.wait_ge(eb_hi_s, nb * KC + c + 1)
                lo_of(eb_lo[:, c, :], e_raw[c % NR][:], eb_hi[:, c, :]).then_inc(eb_lo_s, 1)

            def e_bias(nb, c):
                cs = bass.ds(nb * BW, BW)
                if c:
                    a = (c - 1) % NR
                    v.wait_ge(e_used[a], (nb * 2 + (c - 1) // NR if a < KC - NR else nb) + 1 + 1)
                nc.vector.scalar_tensor_tensor(bacc[:, cs], e_raw[c % NR][:], b0c[:, c:c + 1], bacc[:, cs],
                                               ALU.mult, ALU.add).then_inc(e_used[c % NR], 1)

            def h_sum_(i):
                v.wait_ge(h_cp, i + 1)
                nc.vector.tensor_tensor(hx[i % 2][:], bk[4 + i % 4][:, NX0:2 * NX0], hx[i % 2][:], ALU.add).then_inc(h_sum, 1)

            h_sum_(0)
            for i in range(KC):
                if i + 1 < KC:
                    h_sum_(i + 1)
                v.wait_ge(h_hi, i + 1)
                lo_of(gx[:, i, 2 * E:3 * E], hx[i % 2][:, 0:E], gx[:, i, 3 * E:NGL])
                lo_of(h0_lo[:, i, :], hx[i % 2][:, E:NX0], gx[:, i, NGL:NGL + ER]).then_inc(h_lo, 1)
                e_split(0, i)
                e_bias(0, i)

            def g_out(nb, r, last):
                v.wait_ge(g_hi_s, nb * (KC + 1) + r + 1)
                src, s, i = bk[r % 3], g_lo_s[r % 3], r - 1
                cs = bass.ds(nb * BW, BW)
                if last:
                    w = GM - nb * BW
                    cs = slice(nb * BW, GM)
                    if r == 0:
                        lo_of(p0_lg[:, E:2 * E], src[:, w:BW], p0_lg[:, 0:E])
                        lo_of(p0_lo[:, cs], src[:, 0:w], p0_hi[:, cs]).then_inc(s, 1)
                    else:
                        lo_of(gx[:, i, E:2 * E], src[:, w:BW], gx[:, i, 0:E])
                        lo_of(g_lo[:, i, cs], src[:, 0:w], g_hi[:, i, cs]).then_inc(s, 1)
                elif r == 0:
                    lo_of(p0_lo[:, cs], src[:, 0:BW], p0_hi[:, cs]).then_inc(s, 1)
                else:
                    lo_of(g_lo[:, i, cs], src[:, 0:BW], g_hi[:, i, cs]).then_inc(s, 1)

            with v.Fori(0, NB - 1) as nb:
                for r in range(KC):
                    g_out(nb, r, False)
                for c in range(KC):
                    e_split(nb + 1, c)
                    if c < KC - NR:
                        e_bias(nb + 1, c)
                for c in range(KC - NR, KC):
                    e_bias(nb + 1, c)
                g_out(nb, KC, False)
            for r in range(KC + 1):
                g_out(NB - 1, r, True)
            v.wait_ge(bias_mm, 1)
            nc.vector.tensor_copy(biasv[:, 0:10], bk[7][:, 0:10])
            nc.vector.tensor_copy(biasv[0:E, 10:11], bk[7][0:E, 10:11]).then_inc(bias_ok, 1)

            def x_split(n, u, c, raw):
                v.wait_ge(xs_hi, n * KC + c + 1)
                lo_of(x_lo[u][:, c, :], raw[:], x_hi[u][:, c, :]).then_inc(xs_lo, 1)

            for c in range(KC):
                x_split(0, 0, c, x_first[c])
            v.wait_ge(f_hi, 1)
            lo_of(p1_lg[:, E:2 * E], p1_raw[:, NM1 - E:NM1], p1_lg[:, 0:E])
            lo_of(p1_lo, p1_raw[:, 0:NM1 - E], p1_hi[:, 0:NM1 - E]).then_inc(f_lo, 1)
            v.wait_ge(f_hi, 2)
            lo_of(lb1_lo[:], lb1_raw[:], lb1_hi[:]).then_inc(f_lo, 1)

            TR, H, LOW, MID = bk[4], bk[1], bk[2], bk[3]

            def tile(t, u, more, at_):
                tau = t * 2 + u
                c0 = count[0]

                def route(k):
                    lg, eq, key, one = rt
                    m1, m2, dif, s, r, q = rs4
                    wide = lambda a: a[:].unsqueeze(2).to_broadcast([P, 4, E])
                    v.wait_ge(lgt_mm, tau * 2 + k + 1)
                    link(nc.vector.tensor_copy(lg[:], TR[:, 0:4 * E].rearrange("p (s e) -> p s e", e=E)), at_)

                    def top(m, onehot):
                        link(nc.vector.reduce_max(m[:], lg[:], AX_X), at_)
                        link(nc.vector.tensor_tensor(eq[:], lg[:], wide(m), ALU.is_equal), at_)
                        link(nc.vector.tensor_tensor(key[:], eq[:], rev, ALU.mult), at_)
                        link(nc.vector.reduce_max(q[:], key[:], AX_X), at_)
                        link(nc.vector.tensor_tensor(onehot[:], key[:], wide(q), ALU.is_equal), at_)

                    top(m1, one)
                    link(nc.vector.scalar_tensor_tensor(lg[:], one[:], -BIG, lg[:], ALU.mult, ALU.add), at_)
                    top(m2, eq)
                    v.wait_ge(rex_ok, tau * 2 + k + 1)
                    nc.vector.tensor_tensor(dif[:], m2[:], m1[:], ALU.subtract).then_inc(dif_ok, 1)
                    v.wait_ge(rex_ok, tau * 2 + k + 1 + 1)
                    link(nc.vector.tensor_scalar(s[:], dif[:], 1.0, 0.5, ALU.add, ALU.mult), at_)
                    link(nc.vector.reciprocal(r[:], s[:]), at_)
                    link(nc.vector.tensor_tensor(q[:], r[:], dif[:], ALU.mult), at_)
                    nc.vector.tensor_tensor(one[:], one[:], wide(r), ALU.mult)
                    link(nc.vector.tensor_tensor(key[:], eq[:], wide(q), ALU.mult), at_)
                    flat = lambda a: a[:].rearrange("p s e -> p (s e)").unsqueeze(2).to_broadcast([P, 4 * E, ER // E])
                    nc.vector.tensor_tensor(wrep[:].rearrange("p (n r) -> p n r", r=ER // E), flat(one), flat(key),
                                            ALU.add).then_inc(w_ok, 1)

                def v_split(k, name):
                    v.wait_ge(v_hi, tau * 3 + k + 1)
                    lo_of(mv_lo[name][:], mraw[:], mv_hi[name][:]).then_inc(v_lo, 1)

                route(0)
                v.wait_ge(h0_mm, tau + 1)
                v.wait_ge(wx_ok, tau * 2 + 1)
                nc.vector.tensor_tensor(mraw[:], H[:], wx_sb[:], ALU.mult).then_inc(raw_ok, 1)
                v.wait_ge(raw_ok, tau * 3 + 1 + 1)
                v_split(0, "m0")
                v.wait_ge(low_mm, tau + 1)
                nb_ = TT // SEQ
                ms = mask_s[:, bass.ds(tau * nb_, nb_)].unsqueeze(2).to_broadcast([P, nb_, SEQ])
                nc.vector.scalar_tensor_tensor(mraw[:].rearrange("p (b s) -> p b s", s=SEQ),
                                               LOW[:].rearrange("p (b s) -> p b s", s=SEQ), biasv[:, 8:9], ms,
                                               ALU.add, ALU.mult).then_inc(raw_ok, 1)
                v.wait_ge(raw_ok, tau * 3 + 2 + 1)
                v_split(1, "low")
                route(1)
                v.wait_ge(mid_mm, tau + 1)
                v.wait_ge(wx_ok, tau * 2 + 2)
                nc.vector.scalar_tensor_tensor(mraw[:], MID[:], biasv[:, 9:10], wx_sb[:], ALU.add, ALU.mult).then_inc(raw_ok, 1)
                v.wait_ge(raw_ok, tau * 3 + 3 + 1)
                v_split(2, "mid")
                if more:
                    for m in range(KC):
                        x_split(tau + 1, 1 - u, m, x_raw[m % 2])
                return count[0] - c0

            start = count[0]
            with v.Fori(0, NT // 2 - 1) as t:
                tile(t, 0, True, t * LINKS)
                tile(t, 1, True, t * LINKS)
            assert count[0] - start == LINKS, count[0] - start
            count[0] = start + LINKS * (NT // 2 - 1)
            tile(NT // 2 - 1, 0, True, None)
            tile(NT // 2 - 1, 1, False, None)


LINKS = 2 * 2 * 16


def _layout(i):
    a = {k: np.asarray(v) for k, v in i.items()}
    c = np.ascontiguousarray
    consts = np.zeros((P, C_SLOG), np.float32)
    consts[:, C_ID:C_ID + P] = np.eye(P)
    consts[:, C_REV:C_REV + 32] = np.tile(np.arange(E, 0, -1), 4)
    consts[:, C_NIDX:C_NIDX + 2] = (np.arange(P) // (ER // E))[:, None]
    consts[:LV, C_TRI:C_TRI + LV] = np.triu(np.ones((LV, LV)), 1)
    consts[:LV, C_IOTA:C_IOTA + LV] = np.arange(LV)
    consts[2 * E:4 * E, C_SEL:C_SEL + E] = np.tile(np.eye(E), (2, 1))
    consts[:2 * E, C_SEL + E:C_SEL + 2 * E] = np.tile(np.eye(E), (2, 1))
    return {
        "xT": c(a["x"].reshape(T, D).T),
        "w1": c(a["L1_cond_weight"]),
        "m1t": c(np.concatenate([a["L1_ffn_base_W"].T, a["L1_ffn_lora_A"].transpose(1, 0, 2).reshape(D, ER),
                                 a["L1_ffn_router_W"].T], axis=1)),
        "aallt": c(a["L1_cond_lora_a_weights"].reshape(ER, D).T),
        "bl1": c(a["L1_cond_lora_b_weights"].transpose(1, 0, 2).reshape(D, ER)),
        "wbt": c(a["L0_ffn_W_base"].T),
        "x0t": c(np.concatenate([a["L0_ffn_W_router"].T, a["L0_ffn_A"].reshape(ER, D).T], axis=1)),
        "b0t": c(a["L0_ffn_B"].transpose(1, 0, 2).reshape(D, ER)),
        "lb1": c(a["L1_ffn_lora_B"].reshape(ER, D)),
        "lorabt": c(a["L0_cond_lora_B"].T),
        "loraa": c(a["L0_cond_lora_A"]),
        "wq": c(a["L0_cond_weight"]),
        "cbook": c(a["condB_codebook"]),
        "ids": c(a["itok_B_1_7"]),
        "packed": c(np.concatenate([
            consts,
            a["L0_cond_scale_log"].reshape(KC, P, D // GRP).transpose(1, 0, 2).reshape(P, KC * (D // GRP)),
            a["L0_ffn_b_base"].reshape(KC, P).T,
            a["L1_cond_bias"].reshape(KC, P).T,
            np.repeat(a["L1_cond_scaling_factors"], ER // E)[:, None]], axis=1)),
    }


def kernel(**inputs):
    import concourse.bacc as _bacc
    from concourse.bass_utils import run_bass_kernel_spmd as _run

    nc = _bacc.Bacc("TRN2", target_bir_lowering=False, num_devices=1)
    arrays = _layout(inputs)
    args = [nc.dram_tensor(n, a.shape, mybir.dt.from_np(a.dtype), kind="ExternalInput").ap() for n, a in arrays.items()]
    args.append(nc.dram_tensor("out", (D, T), F32, kind="ExternalOutput").ap())
    args.append(nc.dram_tensor("e_scratch", (D, NE), F32, kind="Internal").ap())
    args.append(nc.dram_tensor("p1_scratch", (P, NM1), F32, kind="Internal").ap())
    build(nc, *args)
    r = _run(nc, [arrays], core_ids=[0])
    return np.ascontiguousarray(r.results[0]["out"].T).reshape(T // SEQ, SEQ, D)
```
